# Optimizing a Trainium2 kernel written in Bass

```python
import numpy as np
import jax
import jax.numpy as jnp

def _softmax(x, axis=-1):
    return jax.nn.softmax(x, axis=axis)
def _gelu(x):
    return jax.nn.gelu(x, approximate=True)
def _silu(x):
    return jax.nn.silu(x)
def _sigmoid(x):
    return jax.nn.sigmoid(x)
def _layernorm(x, axis=-1, eps=1e-5):
    m = jnp.mean(x, axis=axis, keepdims=True)
    v = jnp.var(x, axis=axis, keepdims=True)
    return (x - m) / jnp.sqrt(v + eps)
def _scatter_add(tgt, idx, src, axis=0):
    return tgt.at[idx].add(src)
def _segment_sum(src, seg, n):
    return jax.ops.segment_sum(src, seg, n)

kernel_name = 'mk_adj_resnorm_d1_adj_512_05374a'

def setup_inputs(seed: int = 0):
    np.random.seed(seed)
    _w = jnp.asarray
    def _rec_inputs():
        import jax
        import jax.numpy as jnp
        _gk = jax.random.key(seed)
        x = -0.0002928 + 1 * jax.random.normal(jax.random.fold_in(_gk, 1), (8, 2048, 512), jnp.float32)
        _w = (1.0 + jnp.arange(2048, dtype=jnp.float32)) ** -0.5
        _w = _w / _w.mean()
        _pij = jnp.clip(0.0078125 * _w[:, None] * _w[None, :], 0.0, 1.0)
        _a = jax.random.uniform(jax.random.fold_in(_gk, 2), (8, 2048, 2048)) < _pij
        adj = _a.astype(jnp.int32)
        return x, adj
    x, adj = _rec_inputs()
    def _L0_gnn_setup():
        import jax, jax.numpy as jnp
        import numpy as np
        NEG_INF = -9000000000000000.0
        ALPHA = 0.2
        key = jax.random.key(seed)
        k1, k2, k3, k4, k5 = jax.random.split(key, 5)
        B, N, F_in, F_out, H = (4, 2048, 512, 64, 8)
        x = jax.random.normal(k1, (B, N, F_in), dtype=jnp.float32)
        adj = jax.random.randint(k2, (B, N, N), 0, 2, dtype=jnp.int32)
        W = jax.random.normal(k3, (H, F_in, F_out), dtype=jnp.float32) * (1.0 / np.sqrt(F_in))
        a1 = jax.random.normal(k4, (H, F_out), dtype=jnp.float32) * (1.0 / np.sqrt(2 * F_out))
        a2 = jax.random.normal(k5, (H, F_out), dtype=jnp.float32) * (1.0 / np.sqrt(2 * F_out))
        return {'x': x, 'adj': adj, 'W': W, 'a1': a1, 'a2': a2}
    _L0_gnn_all = _L0_gnn_setup()
    _L0_gnn_in = {k: v for k, v in _L0_gnn_all.items() if k in ('W', 'a1', 'a2', )}
    del _L0_gnn_all

    return {
        "x": x,
        "adj": adj,
        "L0_gnn_W": _L0_gnn_in["W"],
        "L0_gnn_a1": _L0_gnn_in["a1"],
        "L0_gnn_a2": _L0_gnn_in["a2"],
    }

def reference(x, adj, L0_gnn_W, L0_gnn_a1, L0_gnn_a2):
    import jax
    import jax.numpy as jnp
    def _L0_gnn_ref(x, adj, W, a1, a2):
        import jax, jax.numpy as jnp
        import numpy as np
        NEG_INF = -9000000000000000.0
        ALPHA = 0.2
        h = jnp.einsum('bnf,hfo->bhno', x, W)
        s1 = jnp.einsum('bhno,ho->bhn', h, a1)
        s2 = jnp.einsum('bhno,ho->bhn', h, a2)
        e = jax.nn.leaky_relu(s1[..., :, None] + s2[..., None, :], negative_slope=ALPHA)
        mask = (adj > 0)[:, None, :, :]
        attn = jax.nn.softmax(jnp.where(mask, e, NEG_INF), axis=-1)
        h_prime = jnp.einsum('bhnm,bhmo->bhno', attn, h)
        B, H, N, Fo = h_prime.shape
        return jnp.transpose(h_prime, (0, 2, 1, 3)).reshape(B, N, H * Fo)

    x = _layernorm(x + _L0_gnn_ref(x, adj, L0_gnn_W, L0_gnn_a1, L0_gnn_a2), axis=-1)
    return x


_drawn_inputs = setup_inputs


def setup_inputs(seed=0):
    import zlib

    import numpy as np

    out = dict(_drawn_inputs(seed))
    spreads = {}
    factors = {}
    for name, (base, spread) in spreads.items():
        noise = np.random.default_rng([zlib.crc32(name.encode()), seed]).standard_normal(out[name].shape)
        drawn = base * np.exp(spread * noise) if base else spread * noise
        out[name] = jnp.asarray(drawn.astype(out[name].dtype))
    for name, factor in factors.items():
        out[name] = (out[name] * factor).astype(out[name].dtype)
    return out
```

```python
from contextlib import ExitStack

import concourse.bass as bass
from concourse import mybir

P = 128
ALU = mybir.AluOpType
ACT = mybir.ActivationFunctionType
AX = mybir.AxisListType
F32 = mybir.dt.float32
F16 = mybir.dt.float16
BF16 = mybir.dt.bfloat16
FP8 = mybir.dt.float8e4
U32 = mybir.dt.uint32
I32 = mybir.dt.int32
RMAX = bass.bass_isa.ReduceOp.max

SLOPE = 0.2
EPS_LN = 1e-5
SPLIT_TOP = 2.0 ** 14
TINY = 2.0 ** -80
STEEP = 2.0 ** 100

BLK = 512
QUADS = 4
DVE_SLOTS = {1: (3,), 2: (3,), 3: (3,)}


def gat_kernel(nc, x, adj, W, a1, a2, out):
    B, N, F = x.shape
    H, _, O = W.shape
    O1 = O + 1
    FC = F // P
    JC = N // P
    IT = BLK // P
    KB = N // BLK
    JQ = JC // QUADS
    JH = JC // 2
    assert F == H * O == 512 and KB % 2 == 0 and H == 2 * IT == 8 and JC == IT * KB and FC == 4
    PIECES = 2 * IT
    UNITS = KB * H
    NBLK = B * KB

    x_rows = x.rearrange("b n f -> (b n) f")
    adj_rows = adj.rearrange("b i j -> (b i) j")
    out_rows = out.rearrange("b n f -> (b n) f")
    s1_rows = nc.dram_tensor("s1_rows", [NBLK * H, BLK], F32, kind="Internal").ap()

    with ExitStack() as ctx:
        def sb(name, shape, dt):
            return ctx.enter_context(nc.sbuf_tensor(name, shape, dt))

        start = {}

        def sem(name, free=None):
            s = ctx.enter_context(nc.semaphore(name))
            start[s] = 0 if free is None else free + 1
            return s

        def at(signal, count):
            return count + start[signal]

        ps = ctx.enter_context(nc.psum_tensor("ps", [P, 8, 512], F32))
        BANK_T = 4
        BANK_X = 6

        b_hi = sb("b_hi", [P, JC, H, O1], F16)
        b_lo = sb("b_lo", [P, JC, H, O1], F16)
        d_hi = sb("d_hi", [P, JC, H, O1], F16)
        d_lo = sb("d_lo", [P, JC, H, O1], F16)
        maskT = [sb(f"maskT{i}", [P, JC, BLK], FP8) for i in range(2)]
        m_pos = [sb(f"m_pos{i}", [P, JC, BLK], FP8) for i in range(2)]
        m_neg = [sb(f"m_neg{i}", [P, JC, BLK], FP8) for i in range(2)]
        step = [sb(f"step{i}", [P, JQ, BLK], FP8) for i in range(QUADS)]
        s1_bc = [sb(f"s1_bc{i}", [P, BLK], F32) for i in range(2)]
        adj_in = [sb(f"adj_in{i}", [P, JH * P], I32) for i in range(2)]
        adj_bf = [sb(f"adj_bf{i}", [P, JH * P], BF16) for i in range(2)]
        xT = sb("xT", [P, FC, N], F32)
        x_in = [sb(f"x_in{i}", [P, F], F32) for i in range(2)]
        W_sb = sb("W_sb", [P, FC, H * O], F32)
        wa = sb("wa", [P, FC, 32], F32)
        att = sb("att", [P, IT, H * O], F32)
        y = sb("y", [P, IT, F], F32)
        sT = sb("sT", [P, BLK], F32)
        s_col = sb("s_col", [P, JC, 2 * H], F32)
        s2_steep = sb("s2_steep", [P, JC, H], F32)
        s2_rel = sb("s2_rel", [P, JC, H], F32)
        r_in = sb("r_in", [P, JC, H], F32)
        r_row = sb("r_row", [P, JC, H], F32)
        e_b = sb("e_b", [P, JC, H], F32)
        e_d = sb("e_d", [P, JC, H], F32)
        k_b = sb("k_b", [P, JC, H], F32)
        k_d = sb("k_d", [P, JC, H], F32)
        xmax = sb("xmax", [P, JC], F32)
        stat = sb("stat", [P, H + 1], F32)
        stat_all = sb("stat_all", [P, H + 1], F32)
        w_norm = sb("w_norm", [P, 1], F32)
        bound = sb("bound", [P, 1], F32)
        bound_inv = sb("bound_inv", [P, 1], F32)
        kappa = sb("kappa", [P, 1], F32)
        kappa_tiny = sb("kappa_tiny", [P, 1], F32)
        prod = sb("prod", [P, 512], F32)
        x_sum = sb("x_sum", [P, F], F32)
        x_sum_bc = sb("x_sum_bc", [P, F], F32)
        tiny_f = sb("tiny_f", [P, H, O1], F32)
        tiny_part = sb("tiny_part", [P, H, O1], BF16)
        tiny = sb("tiny", [P, H, O1], BF16)
        neg_part = sb("neg_part", [P, IT, O1], F32)
        total = sb("total", [P, IT, O1], F32)
        den_inv = sb("den_inv", [P, IT], F32)
        den_scaled = sb("den_scaled", [P, IT], F32)
        ln_stats = sb("ln_stats", [P, IT, 6], F32)
        ln_mv = sb("ln_mv", [P, IT, 2], F32)
        ln_var = sb("ln_var", [P, IT], F32)
        ln_sd = sb("ln_sd", [P, IT], F32)
        ln_rstd = sb("ln_rstd", [P, IT], F32)
        ident = sb("ident", [P, P], F32)
        ident_bf = sb("ident_bf", [P, P], BF16)
        ones = sb("ones", [P, P], F32)
        ones_bf = sb("ones_bf", [P, P], BF16)

        w_loaded = sem("w_loaded")
        a_loaded = sem("a_loaded")
        adj_loaded = [sem(f"adj_loaded{i}") for i in range(2)]
        x_loaded = [sem(f"x_loaded{i}") for i in range(2)]
        y_loaded = sem("y_loaded")
        s1_stored = sem("s1_stored")
        s1_loaded = [sem(f"s1_loaded{i}") for i in range(2)]
        out_stored = sem("out_stored", free=0)
        consts_made = sem("consts_made")
        ident_made = sem("ident_made")
        ident_step = sem("ident_step")
        setup_step = sem("setup_step")
        w_abs_made = sem("w_abs_made")
        w_abs_summed = sem("w_abs_summed")
        wa_made = sem("wa_made")
        adj_cut = sem("adj_cut", free=2)
        piece_turned = sem("piece_turned", free=2)
        piece_copied = sem("piece_copied", free=2)
        x_turned = sem("x_turned", free=2)
        xT_copied = sem("xT_copied", free=2)
        x_maxed = sem("x_maxed", free=2)
        x_summed = sem("x_summed", free=2)
        sT_summed = sem("sT_summed")
        sT_copied = sem("sT_copied")
        s_turned = sem("s_turned")
        s_col_copied = sem("s_col_copied")
        stat_made = sem("stat_made")
        stat_spread = sem("stat_spread")
        s_rel_made = sem("s_rel_made")
        r_sum_made = sem("r_sum_made")
        bound_step = sem("bound_step")
        exp_made = sem("exp_made")
        den_hi_made = sem("den_hi_made")
        k_made = sem("k_made")
        h_summed = sem("h_summed")
        hi_b_made = sem("hi_b_made")
        hi_d_made = sem("hi_d_made")
        lo_made = sem("lo_made", free=0)
        x_sum_turned = sem("x_sum_turned")
        x_sum_cleared = sem("x_sum_cleared")
        x_sum_spread = sem("x_sum_spread")
        h_mean_summed = sem("h_mean_summed")
        tiny_step = sem("tiny_step")
        tiny_made = sem("tiny_made")
        step_act = sem("step_act", free=QUADS)
        step_dve = sem("step_dve", free=1)
        pos_made = sem("pos_made", free=QUADS)
        neg_made = sem("neg_made", free=0)
        unit_done = sem("unit_done", free=1)
        neg_scaled = sem("neg_scaled")
        unit_read = sem("unit_read", free=1)
        den_inverted = sem("den_inverted")
        den_made = sem("den_made")
        att_made = sem("att_made")
        y_made = sem("y_made", free=0)
        ln_stats_made = sem("ln_stats_made")
        ln_mv_made = sem("ln_mv_made")
        ln_var_made = sem("ln_var_made")
        ln_sd_made = sem("ln_sd_made")
        ln_rstd_made = sem("ln_rstd_made")
        y_normed = sem("y_normed")

        waited = {e.engine: sem(f"waited_{n}") for n, e in (("sp", nc.sync), ("pe", nc.tensor), ("act", nc.scalar),
                                                            ("dve", nc.vector), ("pool", nc.gpsimd))}

        def words(ap):
            return ap.bitcast(U32)

        block_ctx = nc.Block()
        block = ctx.enter_context(block_ctx)

        @block.sync
        def _(sp):
            def load_piece(q, slot, row_tile, n):
                sp.wait_ge(adj_cut, at(adj_cut, q - 1))
                sp.dma_start(adj_in[slot][:], adj_rows[bass.ds(row_tile * P, P), slot * JH * P:(slot + 1) * JH * P]
                             ).then_inc(adj_loaded[slot], 16)

            def load_x(xi, slot, row_tile):
                sp.wait_ge(x_turned, at(x_turned, xi - 1))
                sp.wait_ge(x_maxed, at(x_maxed, xi - 1))
                sp.wait_ge(x_summed, at(x_summed, xi - 1))
                sp.dma_start(x_in[slot][:], x_rows[bass.ds(row_tile * P, P), :]).then_inc(x_loaded[slot], 16)

            def store_block(g):
                sp.wait_ge(y_normed, g + 1)
                sp.dma_start(out_rows[bass.ds((g + NBLK) % NBLK * BLK, BLK), :].rearrange("(t p) f -> p t f", p=P), y[:]
                             ).then_inc(out_stored, 16)

            sp.sem_inc(out_stored, start[out_stored])
            for fc in range(FC):
                sp.dma_start(W_sb[:, fc, :].rearrange("p (h o) -> p h o", h=H),
                             W[:, fc * P:(fc + 1) * P, :].rearrange("h p o -> p h o")).then_inc(w_loaded, 16)
            for n, a in enumerate((a1, a2)):
                sp.dma_start(att[:, n, :], a.rearrange("h o -> (h o)").partition_broadcast(P)).then_inc(a_loaded, 16)
            for i in range(JC):
                if i < PIECES:
                    load_piece(i, i % 2, i // 2, i)
                load_x(i, i % 2, i)

            with sp.Fori(0, B) as b:
                sp.wait_ge(sT_copied, b + 1)
                for k in range(KB):
                    sp.dma_start(s1_rows[bass.ds((b * KB + k) * H, H), :], sT[32 * k:32 * k + H, :]
                                 ).then_inc(s1_stored, 16)
                sp.wait_ge(s1_stored, 16 * KB * (b + 1))
                sp.sem_inc(waited[sp.engine], 1)
                with sp.Fori(0, KB // 2) as k2:
                    for par in range(2):
                        g = b * KB + k2 * 2 + par
                        for h in range(H):
                            sp.wait_ge(step_act, at(step_act, QUADS * (g * H + h - 1)))
                            sp.sem_inc(waited[sp.engine], 1)
                            sp.wait_ge(step_dve, at(step_dve, g * H + h - 1))
                            sp.dma_start(s1_bc[h % 2][:],
                                         s1_rows[bass.ds(g * H + h, 1), :].rearrange("a n -> (a n)").partition_broadcast(P)
                                         ).then_inc(s1_loaded[h % 2], 16)
                            load_piece(PIECES * (g + 1) + h, h % 2, ((g + 1) * IT + h // 2) % (NBLK * IT), 0)
                            if h % 2 == 0:
                                load_x(JC + IT * g + h // 2, (h // 2) % 2, (JC + IT * g + h // 2) % (NBLK * IT))
                            if h == 4:
                                if par:
                                    store_block(g - 1)
                                else:
                                    with sp.If(g > 0):
                                        store_block(g - 1)
                            if h == 5:
                                sp.wait_ge(out_stored, at(out_stored, 16 * g))
                                sp.dma_start(y[:], x_rows[bass.ds(g * BLK, BLK), :].rearrange("(t p) f -> p t f", p=P)
                                             ).then_inc(y_loaded, 16)
            store_block(NBLK - 1)
            sp.wait_ge(out_stored, at(out_stored, 16 * NBLK))
            for slot in range(2):
                sp.wait_ge(adj_loaded[slot], 16 * (NBLK + 1) * IT)
                sp.wait_ge(x_loaded[slot], 16 * (NBLK * IT + JC) // 2)

        @block.tensor
        def _(pe):
            def turn_piece(q, slot):
                pe.wait_ge(piece_copied, at(piece_copied, q - 1))
                pe.wait_ge(adj_cut, at(adj_cut, q + 1))
                bank = ps[:, BANK_T + slot, :].bitcast(BF16)
                for j in range(JH):
                    mm = pe.transpose(bank[:, j * P:(j + 1) * P], adj_bf[slot][:, j * P:(j + 1) * P], ident_bf[:])
                mm.then_inc(piece_turned, 1)

            def turn_x(xi, slot, nth):
                pe.wait_ge(xT_copied, at(xT_copied, xi - 1))
                pe.wait_ge(x_loaded[slot], 16 * (nth + 1))
                for fc in range(FC):
                    mm = pe.transpose(ps[:, BANK_X + slot, fc * P:(fc + 1) * P],
                                      x_in[slot][:, fc * P:(fc + 1) * P], ident[:])
                mm.then_inc(x_turned, 1)

            pe.nop().then_inc(piece_turned, start[piece_turned])
            pe.nop().then_inc(x_turned, start[x_turned])
            pe.nop().then_inc(unit_done, start[unit_done])
            pe.wait_ge(consts_made, 2)
            pe.wait_ge(w_abs_made, 1)
            for fc in range(FC):
                mm = pe.matmul(ps[:, 0, :], ones[:], xT[:, fc, 0:F], start=(fc == 0), stop=(fc == FC - 1))
            mm.then_inc(w_abs_summed, 1)
            for i in range(JC):
                if i < PIECES:
                    turn_piece(i, i % 2)
                turn_x(i, i % 2, i // 2)
            pe.wait_ge(wa_made, 1)

            with pe.Fori(0, B) as b:
                pe.wait_ge(xT_copied, at(xT_copied, JC * (b + 1)))
                for fc in range(FC):
                    for k in range(KB):
                        mm = pe.matmul(ps[32 * k:32 * (k + 1), BANK_X, :], wa[:, fc, :], xT[:, fc, k * BLK:(k + 1) * BLK],
                                       start=(fc == 0), stop=(fc == FC - 1))
                mm.then_inc(sT_summed, 1)
                pe.wait_ge(sT_copied, b + 1)
                for t in range(IT):
                    mm = pe.transpose(ps[:, BANK_X + 1, t * P:(t + 1) * P], sT[:, t * P:(t + 1) * P], ident[:])
                mm.then_inc(s_turned, 1)
                for jc in range(JC):
                    if jc == 1:
                        pe.wait_ge(s_col_copied, b + 1)
                    if jc >= 2:
                        pe.wait_ge(hi_d_made, b * JC + jc - 1)
                    for fc in range(FC):
                        mm = pe.matmul(ps[:, BANK_X + jc % 2, :], xT[:, fc, jc * P:(jc + 1) * P], W_sb[:, fc, :],
                                       start=(fc == 0), stop=(fc == FC - 1))
                    mm.then_inc(h_summed, 1)
                    if jc == 2:
                        pe.wait_ge(x_summed, at(x_summed, JC * (b + 1)))
                        pe.wait_ge(unit_read, at(unit_read, UNITS * b - 1))
                        for fc in range(FC):
                            mm = pe.matmul(ps[:, 0, fc:fc + 1], x_sum[:, fc * P:(fc + 1) * P], ones[:, 0:1],
                                           start=True, stop=True)
                        mm.then_inc(x_sum_turned, 1)
                    if jc == 5:
                        pe.wait_ge(x_sum_spread, b + 1)
                        pe.wait_ge(piece_copied, at(piece_copied, PIECES * (b * KB + 1) - 1))
                        for fc in range(FC):
                            mm = pe.matmul(ps[:, BANK_T, :], x_sum_bc[:, fc * P:(fc + 1) * P], W_sb[:, fc, :],
                                           start=(fc == 0), stop=(fc == FC - 1))
                        mm.then_inc(h_mean_summed, 1)
                pe.wait_ge(tiny_made, b + 1)
                pe.wait_ge(lo_made, at(lo_made, 2 * JC * (b + 1)))
                pe.sem_inc(waited[pe.engine], 1)
                with pe.Fori(0, KB // 2) as k2:
                    for par in range(2):
                        g = b * KB + k2 * 2 + par
                        for h in range(H):
                            u = g * H + h
                            turn_piece(PIECES * (g + 1) + h, h % 2)
                            if h % 2 == 0:
                                turn_x(JC + IT * g + h // 2, (h // 2) % 2, JC // 2 + g * (IT // 2) + h // 4)
                            pe.wait_ge(neg_made, at(neg_made, QUADS * (u + 1)))
                            pe.wait_ge(unit_read, at(unit_read, u - 1))
                            hp = h % 2
                            for it in range(IT):
                                acc_pos = ps[:, 2 * hp, it * O1:(it + 1) * O1]
                                acc_neg = ps[:, 2 * hp + 1, it * O1:(it + 1) * O1]
                                rows = slice(it * P, (it + 1) * P)
                                pe.matmul(acc_pos, ones_bf[:], tiny[:, h, :], start=True, stop=False)
                                for j in range(JC):
                                    last = j == JC - 1
                                    pe.matmul(acc_pos, m_pos[hp][:, j, rows], b_hi[:, j, h, :], start=False, stop=False)
                                    pe.matmul(acc_pos, m_pos[hp][:, j, rows], b_lo[:, j, h, :], start=False, stop=last)
                                    pe.matmul(acc_neg, m_neg[hp][:, j, rows], d_hi[:, j, h, :], start=(j == 0), stop=False)
                                    mm = pe.matmul(acc_neg, m_neg[hp][:, j, rows], d_lo[:, j, h, :], start=False, stop=last)
                            mm.then_inc(unit_done, 1)

        @block.scalar
        def _(act):
            def copy_piece(q, slot, buf, it):
                act.wait_ge(piece_turned, at(piece_turned, q + 1))
                act.sem_inc(waited[act.engine], 1)
                bank = ps[:, BANK_T + slot, :].bitcast(BF16).rearrange("p (j i) -> p j i", j=JH)
                nc.scalar.activation(maskT[buf][:, slot * JH:(slot + 1) * JH, it * P:(it + 1) * P], bank, ACT.Copy,
                                     saturate=False).then_inc(piece_copied, 1)

            def copy_xT(xi, slot, col):
                act.wait_ge(x_turned, at(x_turned, xi + 1))
                bank = ps[:, BANK_X + slot, :].rearrange("p (c n) -> p c n", c=FC)
                nc.scalar.activation(xT[:, :, bass.ds(col, P)], bank, ACT.Copy).then_inc(xT_copied, 1)

            act.nop().then_inc(piece_copied, start[piece_copied])
            act.nop().then_inc(xT_copied, start[xT_copied])
            act.nop().then_inc(step_act, start[step_act])
            act.wait_ge(w_abs_summed, 1)
            for i in range(JC):
                if i < PIECES - 1:
                    copy_piece(i, i % 2, 0, i // 2)
                copy_xT(i, i % 2, i * P)

            with act.Fori(0, B) as b:
                act.wait_ge(sT_summed, b + 1)
                nc.scalar.activation(sT[:], ps[:, BANK_X, :], ACT.Copy).then_inc(sT_copied, 1)
                act.wait_ge(s_rel_made, b + 1)
                nc.scalar.activation(e_b[:], s2_rel[:], ACT.Exp)
                nc.scalar.activation(e_d[:], s2_rel[:], ACT.Exp, scale=SLOPE)
                nc.scalar.activation(r_row[:], r_in[:], ACT.Exp, scale=SLOPE - 1.0).then_inc(exp_made, 1)
                with act.Fori(0, KB // 2) as k2:
                    for par in range(2):
                        g = b * KB + k2 * 2 + par
                        for h in range(H):
                            u = g * H + h
                            prev = (h - 1) % PIECES
                            buf = par if h == 0 else 1 - par
                            act.wait_ge(neg_made, at(neg_made, QUADS * H * g))
                            copy_piece(PIECES * (g + 1) + h - 1, prev % 2, buf, prev // 2)
                            if h % 2 == 1:
                                t = h // 2
                                act.wait_ge(h_summed, JC * (b + 1))
                                copy_xT(JC + IT * g + t, t % 2, k2 * (2 * BLK) + par * BLK + t * P)
                            act.wait_ge(s1_loaded[h % 2], 16 * (g * (H // 2) + h // 2 + 1))
                            for qd in range(QUADS):
                                act.wait_ge(pos_made, at(pos_made, QUADS * (u - 1) + qd + 1))
                                act.sem_inc(waited[act.engine], 1)
                                mine = [c for c in range(JQ) if c not in DVE_SLOTS.get(qd, ())]
                                for c in mine:
                                    j = qd * JQ + c
                                    ins = nc.scalar.activation(step[qd][:, c, :], s1_bc[h % 2][:], ACT.Relu,
                                                               bias=s2_steep[:, j, h:h + 1], scale=STEEP, saturate=False)
                                ins.then_inc(step_act, 1)
                            if h == 2:
                                def deviation():
                                    act.wait_ge(ln_var_made, g)
                                    nc.scalar.activation(ln_sd[:], ln_var[:], ACT.Sqrt).then_inc(ln_sd_made, 1)
                                if par:
                                    deviation()
                                else:
                                    with act.If(g > 0):
                                        deviation()
            act.wait_ge(ln_var_made, NBLK)
            nc.scalar.activation(ln_sd[:], ln_var[:], ACT.Sqrt).then_inc(ln_sd_made, 1)
            act.wait_ge(piece_turned, at(piece_turned, PIECES * (NBLK + 1)))

        @block.vector
        def _(dve):
            V = nc.vector

            def cut_piece(q, slot, nth):
                dve.wait_ge(adj_loaded[slot], 16 * (nth + 1))
                dve.wait_ge(piece_turned, at(piece_turned, q - 1))
                V.tensor_scalar(adj_bf[slot][:], adj_in[slot][:], 0.0, None, ALU.is_gt).then_inc(adj_cut, 1)

            def max_x(xi, slot, nth, col):
                dve.wait_ge(x_loaded[slot], 16 * (nth + 1))
                V.tensor_reduce(xmax[:, bass.ds(col, 1)], x_in[slot][:], AX.X, ALU.max,
                                apply_absolute_value=True).then_inc(x_maxed, 1)

            def take_unit(u, h, it0, g):
                hp = h % 2
                pos = ps[:, 2 * hp, 0:IT * O1].rearrange("p (t c) -> p t c", t=IT)
                neg = ps[:, 2 * hp + 1, 0:IT * O1].rearrange("p (t c) -> p t c", t=IT)
                r = r_row[:, bass.ds(it0, IT), h:h + 1].to_broadcast([P, IT, O1])
                dve.wait_ge(unit_done, at(unit_done, u + 1))
                V.tensor_tensor(neg_part[:], neg, r, ALU.mult).then_inc(neg_scaled, 1)
                dve.wait_ge(neg_scaled, u + 1)
                V.tensor_tensor(total[:], pos, neg_part[:], ALU.add).then_inc(unit_read, 1)
                dve.wait_ge(unit_read, at(unit_read, u + 1))
                V.reciprocal(den_inv[:], total[:, :, O]).then_inc(den_inverted, 1)
                dve.wait_ge(den_inverted, u + 1)
                V.tensor_scalar(den_scaled[:], den_inv[:], bound[:, 0:1], None, ALU.mult).then_inc(den_made, 1)
                dve.wait_ge(den_made, u + 1)
                if h == 0:
                    dve.wait_ge(y_made, at(y_made, 2 * g))
                ins = V.tensor_tensor(att[:, :, h * O:(h + 1) * O], total[:, :, 0:O],
                                      den_scaled[:].unsqueeze(2).to_broadcast([P, IT, O]), ALU.mult)
                if h == H - 1:
                    ins.then_inc(att_made, 1)

            def ln_statistics(g):
                dve.wait_ge(y_made, at(y_made, 2 * (g + 1)))
                for t in range(IT):
                    ins = V.bn_stats(ln_stats[:, t, :], y[:, t, :])
                ins.then_inc(ln_stats_made, 1)
                dve.wait_ge(ln_stats_made, g + 1)
                dve.sem_inc(waited[dve.engine], 1)
                for t in range(IT):
                    ins = V.bn_aggr(ln_mv[:, t, :], ln_stats[:, t, :])
                ins.then_inc(ln_mv_made, 1)
                dve.wait_ge(ln_mv_made, g + 1)
                V.tensor_scalar(ln_var[:], ln_mv[:, :, 1], EPS_LN, None, ALU.add).then_inc(ln_var_made, 1)

            def ln_apply(g):
                dve.wait_ge(ln_sd_made, g + 1)
                V.reciprocal(ln_rstd[:], ln_sd[:]).then_inc(ln_rstd_made, 1)
                dve.wait_ge(ln_rstd_made, g + 1)
                for t in range(IT):
                    ins = V.tensor_scalar(y[:, t, :], y[:, t, :], ln_mv[:, t, 0:1], ln_rstd[:, t:t + 1],
                                          ALU.subtract, ALU.mult)
                ins.then_inc(y_normed, 1)

            V.nop().then_inc(adj_cut, start[adj_cut])
            V.nop().then_inc(x_maxed, start[x_maxed])
            V.nop().then_inc(step_dve, start[step_dve])
            V.nop().then_inc(pos_made, start[pos_made])
            V.nop().then_inc(neg_made, start[neg_made])
            V.nop().then_inc(unit_read, start[unit_read])
            V.memset(ones_bf[:], 1.0)
            V.memset(wa[:], 0.0)
            V.memset(tiny_f[:], TINY * SPLIT_TOP).then_inc(setup_step, 1)
            dve.wait_ge(ident_made, 1)
            V.tensor_copy(ident_bf[:], ident[:]).then_inc(consts_made, 1)
            dve.wait_ge(w_loaded, 16 * FC)
            dve.wait_ge(a_loaded, 32)
            done = 1
            for n in range(2):
                for fc in range(FC):
                    dve.wait_ge(setup_step, done)
                    V.tensor_tensor(prod[:], W_sb[:, fc, :], att[:, n, :], ALU.mult).then_inc(setup_step, 1)
                    done += 1
                    dve.wait_ge(setup_step, done)
                    ins = V.tensor_reduce(wa[:, fc, n * H:(n + 1) * H], prod[:].rearrange("p (h o) -> p h o", h=H),
                                          AX.X, ALU.add)
                    ins.then_inc(setup_step, 1)
                    done += 1
            dve.wait_ge(setup_step, done)
            V.nop().then_inc(wa_made, 1)
            for fc in range(FC):
                ins = V.scalar_tensor_tensor(out=xT[:, fc, 0:F], in0=W_sb[:, fc, :], scalar=-1.0, in1=W_sb[:, fc, :],
                                             op0=ALU.mult, op1=ALU.max)
            ins.then_inc(w_abs_made, 1)
            dve.wait_ge(w_abs_summed, 1)
            V.tensor_reduce(w_norm[:], ps[:, 0, :], AX.X, ALU.max)
            for i in range(JC):
                if i < PIECES:
                    cut_piece(i, i % 2, i // 2)
                max_x(i, i % 2, i // 2, i)

            def batch_start(b):
                dve.wait_ge(s_turned, b + 1)
                V.tensor_copy(s_col[:].rearrange("p (k t) s -> p t k s", t=IT),
                              ps[:, BANK_X + 1, :].rearrange("p (t k s) -> p t k s", t=IT, k=KB)[:, :, :, 0:2 * H]
                              ).then_inc(s_col_copied, 1)
                dve.wait_ge(s_col_copied, b + 1)
                dve.wait_ge(x_maxed, at(x_maxed, JC * (b + 1)))
                s1 = s_col[:, :, 0:H]
                s2 = s_col[:, :, H:2 * H]
                V.tensor_reduce(stat[:, 0:H], s2.rearrange("p j k -> p k j"), AX.X, ALU.max)
                V.tensor_reduce(stat[:, H:H + 1], xmax[:], AX.X, ALU.max).then_inc(stat_made, 1)
                V.tensor_scalar(s2_steep[:], s2, STEEP, None, ALU.mult)
                dve.wait_ge(stat_spread, b + 1)
                top = stat_all[:, 0:H].unsqueeze(1).to_broadcast([P, JC, H])
                V.tensor_tensor(s2_rel[:], s2, top, ALU.subtract)
                V.tensor_tensor(r_in[:], s1, top, ALU.add).then_inc(r_sum_made, 1)
                V.tensor_scalar(bound[:], stat_all[:, H:H + 1], w_norm[:, 0:1], 1e-20, ALU.mult, ALU.max
                                ).then_inc(bound_step, 1)
                dve.wait_ge(r_sum_made, b + 1)
                V.tensor_scalar(r_in[:], r_in[:], 0.0, None, ALU.max).then_inc(s_rel_made, 1)
                dve.wait_ge(bound_step, 3 * b + 1)
                V.reciprocal(bound_inv[:], bound[:]).then_inc(bound_step, 1)
                dve.wait_ge(bound_step, 3 * b + 2)
                V.tensor_scalar(kappa[:], bound_inv[:], SPLIT_TOP, None, ALU.mult)
                V.tensor_scalar(kappa_tiny[:], bound_inv[:], SPLIT_TOP * TINY / N, None, ALU.mult
                                ).then_inc(bound_step, 1)
                dve.wait_ge(bound_step, 3 * b + 3)
                dve.wait_ge(exp_made, b + 1)
                V.tensor_scalar(b_hi[:, :, :, O], e_b[:], SPLIT_TOP, None, ALU.mult)
                V.tensor_scalar(d_hi[:, :, :, O], e_d[:], SPLIT_TOP, None, ALU.mult).then_inc(den_hi_made, 1)
                V.tensor_scalar(k_b[:], e_b[:], kappa[:, 0:1], None, ALU.mult)
                V.tensor_scalar(k_d[:], e_d[:], kappa[:, 0:1], None, ALU.mult).then_inc(k_made, 1)
                dve.wait_ge(den_hi_made, b + 1)
                V.scalar_tensor_tensor(out=b_lo[:, :, :, O], in0=e_b[:], scalar=SPLIT_TOP, in1=b_hi[:, :, :, O],
                                       op0=ALU.mult, op1=ALU.subtract)
                V.scalar_tensor_tensor(out=d_lo[:, :, :, O], in0=e_d[:], scalar=SPLIT_TOP, in1=d_hi[:, :, :, O],
                                       op0=ALU.mult, op1=ALU.subtract)
                dve.wait_ge(k_made, b + 1)

            def split_chunk(b, jc):
                bank = ps[:, BANK_X + jc % 2, :].rearrange("p (h o) -> p h o", h=H)
                full = prod[:].rearrange("p (h o) -> p h o", h=H)
                kb = k_b[:, jc, :].unsqueeze(2).to_broadcast([P, H, O])
                kd = k_d[:, jc, :].unsqueeze(2).to_broadcast([P, H, O])
                dve.wait_ge(h_summed, b * JC + jc + 1)
                V.tensor_tensor(b_hi[:, jc, :, 0:O], bank, kb, ALU.mult)
                dve.wait_ge(lo_made, at(lo_made, 2 * JC * b + 2 * jc))
                V.tensor_tensor(full, bank, kb, ALU.mult).then_inc(hi_b_made, 1)
                V.tensor_tensor(d_hi[:, jc, :, 0:O], bank, kd, ALU.mult)
                dve.wait_ge(lo_made, at(lo_made, 2 * JC * b + 2 * jc + 1))
                V.tensor_tensor(full, bank, kd, ALU.mult).then_inc(hi_d_made, 1)

            def no_edge_term(b):
                n = 6 * b
                dve.wait_ge(h_mean_summed, b + 1)
                V.tensor_scalar(tiny_f[:, :, 0:O], ps[:, BANK_T, :].rearrange("p (h o) -> p h o", h=H),
                                kappa_tiny[:, 0:1], None, ALU.mult)
                V.memset(tiny_f[:, :, O:O1], TINY * SPLIT_TOP).then_inc(tiny_step, 1)
                dve.wait_ge(tiny_step, n + 1)
                for part in range(3):
                    V.tensor_copy(tiny_part[:], tiny_f[:]).then_inc(tiny_step, 1)
                    dve.wait_ge(tiny_step, n + 2 + 2 * part)
                    if part == 0:
                        V.tensor_scalar(tiny[:], tiny_part[:], ident[:, 0:1], None, ALU.mult)
                    else:
                        ins = V.scalar_tensor_tensor(out=tiny[:], in0=tiny_part[:], scalar=ident[:, part:part + 1],
                                                     in1=tiny[:], op0=ALU.mult, op1=ALU.add)
                    if part < 2:
                        V.tensor_tensor(tiny_f[:], tiny_f[:], tiny_part[:], ALU.subtract).then_inc(tiny_step, 1)
                        dve.wait_ge(tiny_step, n + 3 + 2 * part)
                ins.then_inc(tiny_made, 1)

            with dve.Fori(0, B) as b:
                with dve.If(b > 0):
                    take_unit(b * UNITS - 1, H - 1, (KB - 1) * IT, b * KB - 1)
                batch_start(b)
                for jc in range(JC):
                    split_chunk(b, jc)
                    if jc == 3:
                        dve.wait_ge(x_sum_turned, b + 1)
                        for fc in range(FC):
                            ins = V.tensor_scalar(x_sum_bc[:, fc * P:(fc + 1) * P], ones[:], ps[:, 0, fc:fc + 1], None,
                                                  ALU.mult)
                        ins.then_inc(x_sum_spread, 1)
                    if jc == 8:
                        no_edge_term(b)
                with dve.Fori(0, KB // 2) as k2:
                    for par in range(2):
                        g = b * KB + k2 * 2 + par
                        for h in range(H):
                            u = g * H + h
                            hp = h % 2
                            cut_piece(PIECES * (g + 1) + h, h % 2, (g + 1) * IT + h // 2)
                            if h % 2 == 0:
                                t = h // 2
                                max_x(JC + IT * g + t, t % 2, JC // 2 + g * (IT // 2) + h // 4,
                                      k2 * (2 * IT) + par * IT + t)
                            dve.wait_ge(s1_loaded[hp], 16 * (g * (H // 2) + h // 2 + 1))
                            dve.sem_inc(waited[dve.engine], 1)
                            for qd, chunks in DVE_SLOTS.items():
                                for c in chunks:
                                    j = qd * JQ + c
                                    ins = V.tensor_scalar(step[qd][:, c, :], s1_bc[hp][:], s_col[:, j, H + h:H + h + 1],
                                                          0.0, ALU.add, ALU.is_gt, saturate=False)
                            ins.then_inc(step_dve, 1)
                            if h == 0:
                                dve.wait_ge(piece_copied, at(piece_copied, PIECES * (g + 1)))
                            dve.wait_ge(unit_done, at(unit_done, u - 1))
                            for qd in range(QUADS + 1):
                                if qd < QUADS:
                                    dve.wait_ge(step_act, at(step_act, QUADS * u + qd + 1))
                                    if qd == 0:
                                        dve.wait_ge(step_dve, at(step_dve, u + 1))
                                    js = slice(qd * JQ, (qd + 1) * JQ)
                                    V.tensor_tensor(words(m_pos[hp][:, js, :]), words(step[qd][:]),
                                                    words(maskT[par][:, js, :]), ALU.bitwise_and).then_inc(pos_made, 1)
                                if qd > 0:
                                    js = slice((qd - 1) * JQ, qd * JQ)
                                    dve.wait_ge(pos_made, at(pos_made, QUADS * u + qd))
                                    V.tensor_tensor(words(m_neg[hp][:, js, :]), words(m_pos[hp][:, js, :]),
                                                    words(maskT[par][:, js, :]), ALU.bitwise_xor).then_inc(neg_made, 1)
                            if h > 0:
                                take_unit(u - 1, h - 1, k2 * (2 * IT) + par * IT, g)
                            elif par:
                                take_unit(u - 1, H - 1, k2 * (2 * IT), g - 1)
                            else:
                                with dve.If(k2 > 0):
                                    take_unit(u - 1, H - 1, (k2 * (2 * IT) + JC - IT) % JC, g - 1)
                            for when, work in ((1, ln_statistics), (3, ln_apply)):
                                if h == when:
                                    if par:
                                        work(g - 1)
                                    else:
                                        with dve.If(g > 0):
                                            work(g - 1)
            take_unit(B * UNITS - 1, H - 1, (KB - 1) * IT, NBLK - 1)
            ln_statistics(NBLK - 1)
            ln_apply(NBLK - 1)

        @block.gpsimd
        def _(pool):
            G = nc.gpsimd

            def add_x(xi, slot, nth):
                pool.wait_ge(x_summed, at(x_summed, xi))
                pool.wait_ge(x_loaded[slot], 16 * (nth + 1))
                G.tensor_tensor(x_sum[:], x_sum[:], x_in[slot][:], ALU.add).then_inc(x_summed, 1)

            def residual(g):
                pool.wait_ge(y_loaded, 16 * (g + 1))
                pool.wait_ge(att_made, g + 1)
                for half in range(2):
                    t = slice(half * IT // 2, (half + 1) * IT // 2)
                    G.tensor_tensor(y[:, t, :], y[:, t, :], att[:, t, :], ALU.add).then_inc(y_made, 1)

            G.memset(ones[:], 1.0)
            G.memset(x_sum[:], 0.0)
            G.memset(ident[:], 0.0).then_inc(ident_step, 1)
            pool.wait_ge(ident_step, 1)
            G.affine_select(out=ident[:], in_=ident[:], compare_op=ALU.not_equal, fill=1.0, base=0,
                            pattern=[[-1, P]], channel_multiplier=1).then_inc(ident_made, 1)
            pool.wait_ge(ident_made, 1)
            G.nop().then_inc(consts_made, 1)
            G.nop().then_inc(x_summed, start[x_summed])
            G.nop().then_inc(lo_made, start[lo_made])
            G.nop().then_inc(y_made, start[y_made])
            for i in range(JC):
                add_x(i, i % 2, i // 2)

            with pool.Fori(0, B) as b:
                pool.wait_ge(stat_made, b + 1)
                pool.sem_inc(waited[pool.engine], 1)
                G.partition_all_reduce(stat_all[:], stat[:], P, RMAX).then_inc(stat_spread, 1)
                for jc in range(JC):
                    full = prod[:].rearrange("p (h o) -> p h o", h=H)
                    pool.wait_ge(hi_b_made, b * JC + jc + 1)
                    G.tensor_tensor(b_lo[:, jc, :, 0:O], full, b_hi[:, jc, :, 0:O], ALU.subtract).then_inc(lo_made, 1)
                    pool.wait_ge(hi_d_made, b * JC + jc + 1)
                    G.tensor_tensor(d_lo[:, jc, :, 0:O], full, d_hi[:, jc, :, 0:O], ALU.subtract).then_inc(lo_made, 1)
                    if jc == 4:
                        pool.wait_ge(x_sum_turned, b + 1)
                        pool.sem_inc(waited[pool.engine], 1)
                        G.memset(x_sum[:], 0.0).then_inc(x_sum_cleared, 1)
                pool.wait_ge(x_sum_cleared, b + 1)
                pool.sem_inc(waited[pool.engine], 1)
                with pool.Fori(0, KB // 2) as k2:
                    for par in range(2):
                        g = b * KB + k2 * 2 + par
                        for t in range(IT):
                            add_x(JC + IT * g + t, t % 2, JC // 2 + g * (IT // 2) + t // 2)
                            if t == 0:
                                if par:
                                    residual(g - 1)
                                else:
                                    with pool.If(g > 0):
                                        residual(g - 1)
            residual(NBLK - 1)


_INS = ["x", "adj", "L0_gnn_W", "L0_gnn_a1", "L0_gnn_a2"]


def kernel(**inputs):
    import numpy as _np
    import concourse.bacc as _bacc
    from concourse import mybir as _mybir
    from concourse.bass_utils import run_bass_kernel_spmd as _run

    nc = _bacc.Bacc("TRN2", target_bir_lowering=False, num_devices=1, dynamic_dma_scratch_size=1024)
    arrays, args = {}, []
    for name in _INS:
        a = _np.ascontiguousarray(inputs[name])
        arrays[f"in_{name}"] = a
        args.append(nc.dram_tensor(f"in_{name}", a.shape, _mybir.dt.from_np(a.dtype), kind="ExternalInput").ap())
    shape = arrays["in_x"].shape
    args.append(nc.dram_tensor("out_0", shape, _mybir.dt.float32, kind="ExternalOutput").ap())
    gat_kernel(nc, *args)
    r = _run(nc, [arrays], core_ids=[0])
    return r.results[0]["out_0"]
```

```python
from contextlib import ExitStack

import concourse.bass as bass
from concourse import mybir

P = 128
ALU = mybir.AluOpType
ACT = mybir.ActivationFunctionType
AX = mybir.AxisListType
F32 = mybir.dt.float32
F16 = mybir.dt.float16
BF16 = mybir.dt.bfloat16
FP8 = mybir.dt.float8e4
U32 = mybir.dt.uint32
I32 = mybir.dt.int32
RMAX = bass.bass_isa.ReduceOp.max

SLOPE = 0.2
EPS_LN = 1e-5
SPLIT_TOP = 2.0 ** 14
TINY = 2.0 ** -80
STEEP = 2.0 ** 100

BLK = 512
QUADS = 4
DVE_SLOTS = {0: (3,), 1: (3,), 2: (3,), 3: (3,)}

PIECES_OF = ((0, 1), (2,), (3,), (4,), (5,), (6,), (7,), ())


def pieces_ahead(h, ahead):
    later, unit = divmod(h + ahead, len(PIECES_OF))
    return [(later, i) for i in PIECES_OF[unit]]


def gat_kernel(nc, x, adj, W, a1, a2, out):
    B, N, F = x.shape
    H, _, O = W.shape
    O1 = O + 1
    FC = F // P
    JC = N // P
    IT = BLK // P
    KB = N // BLK
    JQ = JC // QUADS
    JH = JC // 2
    assert F == H * O == 512 and KB % 2 == 0 and H == 2 * IT == 8 and JC == IT * KB and FC == 4
    PIECES = 2 * IT
    UNITS = KB * H
    NBLK = B * KB

    x_rows = x.rearrange("b n f -> (b n) f")
    adj_rows = adj.rearrange("b i j -> (b i) j")
    out_rows = out.rearrange("b n f -> (b n) f")
    s1_rows = nc.dram_tensor("s1_rows", [NBLK * H, BLK], F32, kind="Internal").ap()

    with ExitStack() as ctx:
        def sb(name, shape, dt):
            return ctx.enter_context(nc.sbuf_tensor(name, shape, dt))

        start = {}

        def sem(name, free=None):
            s = ctx.enter_context(nc.semaphore(name))
            start[s] = 0 if free is None else free + 1
            return s

        def at(signal, count):
            return count + start[signal]

        ps = ctx.enter_context(nc.psum_tensor("ps", [P, 8, 512], F32))
        BANK_T = 4
        BANK_X = 6

        b_hi = sb("b_hi", [P, JC, H, O1], F16)
        b_lo = sb("b_lo", [P, JC, H, O1], F16)
        d_hi = sb("d_hi", [P, JC, H, O1], F16)
        d_lo = sb("d_lo", [P, JC, H, O1], F16)
        maskT = [sb(f"maskT{i}", [P, JC, BLK], FP8) for i in range(2)]
        m_pos = [sb(f"m_pos{i}", [P, JC, BLK], FP8) for i in range(2)]
        m_neg = [sb(f"m_neg{i}", [P, JC, BLK], FP8) for i in range(2)]
        step = [sb(f"step{i}", [P, JQ, BLK], FP8) for i in range(QUADS)]
        s1_bc = [sb(f"s1_bc{i}", [P, BLK], F32) for i in range(2)]
        adj_in = [sb(f"adj_in{i}", [P, JH * P], I32) for i in range(2)]
        adj_bf = [sb(f"adj_bf{i}", [P, JH * P], BF16) for i in range(2)]
        xT = sb("xT", [P, FC, N], F32)
        x_in = [sb(f"x_in{i}", [P, F], F32) for i in range(2)]
        W_sb = sb("W_sb", [P, FC, H * O], F32)
        wa = sb("wa", [P, FC, 32], F32)
        att = sb("att", [P, IT, H * O], F32)
        y = sb("y", [P, IT, F], F32)
        sT = sb("sT", [P, BLK], F32)
        s_col = sb("s_col", [P, JC, 2 * H], F32)
        s2_steep = sb("s2_steep", [P, JC, H], F32)
        s2_rel = sb("s2_rel", [P, JC, H], F32)
        r_in = sb("r_in", [P, JC, H], F32)
        r_row = sb("r_row", [P, JC, H], F32)
        e_b = sb("e_b", [P, JC, H], F32)
        e_d = sb("e_d", [P, JC, H], F32)
        k_b = sb("k_b", [P, JC, H], F32)
        k_d = sb("k_d", [P, JC, H], F32)
        xmax = sb("xmax", [P, JC], F32)
        stat = sb("stat", [P, H + 1], F32)
        stat_all = sb("stat_all", [P, H + 1], F32)
        w_norm = sb("w_norm", [P, 1], F32)
        bound = sb("bound", [P, 1], F32)
        bound_inv = sb("bound_inv", [P, 1], F32)
        kappa = sb("kappa", [P, 1], F32)
        kappa_tiny = sb("kappa_tiny", [P, 1], F32)
        prod = sb("prod", [P, 512], F32)
        prod_d = sb("prod_d", [P, 512], F32)
        x_sum = sb("x_sum", [P, F], F32)
        x_sum_bc = sb("x_sum_bc", [P, F], F32)
        tiny_f = sb("tiny_f", [P, H, O1], F32)
        tiny_part = sb("tiny_part", [P, H, O1], BF16)
        tiny = sb("tiny", [P, H, O1], BF16)
        neg_part = sb("neg_part", [P, IT, O1], F32)
        total = [sb(f"total{i}", [P, IT, O1], F32) for i in range(2)]
        den_inv = [sb(f"den_inv{i}", [P, IT], F32) for i in range(2)]
        den_scaled = [sb(f"den_scaled{i}", [P, IT], F32) for i in range(2)]
        ln_stats = sb("ln_stats", [P, IT, 6], F32)
        ln_mv = sb("ln_mv", [P, IT, 2], F32)
        ln_var = sb("ln_var", [P, IT], F32)
        minus_half = sb("minus_half", [P, IT], F32)
        ln_rstd = sb("ln_rstd", [P, IT], F32)
        ident = sb("ident", [P, P], F32)
        ident_bf = sb("ident_bf", [P, P], BF16)
        ones = sb("ones", [P, P], F32)
        ones_bf = sb("ones_bf", [P, P], BF16)

        w_loaded = sem("w_loaded")
        a_loaded = sem("a_loaded")
        adj_loaded = [sem(f"adj_loaded{i}") for i in range(2)]
        x_loaded = [sem(f"x_loaded{i}") for i in range(2)]
        y_loaded = sem("y_loaded")
        s1_stored = sem("s1_stored")
        s1_loaded = [sem(f"s1_loaded{i}") for i in range(2)]
        out_stored = sem("out_stored", free=0)
        consts_made = sem("consts_made")
        ident_made = sem("ident_made")
        ident_step = sem("ident_step")
        setup_step = sem("setup_step")
        w_abs_made = sem("w_abs_made")
        w_abs_summed = sem("w_abs_summed")
        wa_made = sem("wa_made")
        adj_cut = sem("adj_cut", free=2)
        piece_turned = sem("piece_turned", free=2)
        piece_copied = sem("piece_copied", free=2)
        x_turned = sem("x_turned", free=2)
        xT_copied = sem("xT_copied", free=2)
        x_maxed = sem("x_maxed", free=2)
        x_summed = sem("x_summed", free=2)
        sT_summed = sem("sT_summed")
        sT_copied = sem("sT_copied")
        s_turned = sem("s_turned")
        s_col_copied = sem("s_col_copied")
        stat_made = sem("stat_made")
        stat_spread = sem("stat_spread")
        s_rel_made = sem("s_rel_made")
        r_sum_made = sem("r_sum_made")
        bound_step = sem("bound_step")
        exp_made = sem("exp_made")
        den_hi_made = sem("den_hi_made")
        k_made = sem("k_made")
        h_summed = sem("h_summed")
        hi_b_made = sem("hi_b_made")
        hi_d_made = sem("hi_d_made")
        lo_made = sem("lo_made", free=1)
        x_sum_turned = sem("x_sum_turned")
        x_sum_cleared = sem("x_sum_cleared")
        x_sum_spread = sem("x_sum_spread")
        h_mean_summed = sem("h_mean_summed")
        tiny_step = sem("tiny_step")
        tiny_made = sem("tiny_made")
        step_act = sem("step_act", free=QUADS)
        step_dve = sem("step_dve", free=1)
        pos_made = sem("pos_made", free=QUADS)
        neg_made = sem("neg_made", free=0)
        unit_done = sem("unit_done", free=1)
        pos_summed = sem("pos_summed", free=1)
        neg_scaled = sem("neg_scaled")
        unit_read = sem("unit_read", free=1)
        den_inverted = sem("den_inverted")
        den_made = sem("den_made")
        att_made = sem("att_made", free=1)
        y_made = sem("y_made", free=0)
        ln_stats_made = sem("ln_stats_made")
        ln_mv_made = sem("ln_mv_made")
        ln_var_made = sem("ln_var_made")
        ln_rstd_made = sem("ln_rstd_made")
        y_normed = sem("y_normed")

        waited = {e.engine: sem(f"waited_{n}") for n, e in (("sp", nc.sync), ("pe", nc.tensor), ("act", nc.scalar),
                                                            ("dve", nc.vector), ("pool", nc.gpsimd))}

        def words(ap):
            return ap.bitcast(U32)

        block = ctx.enter_context(nc.Block())

        @block.sync
        def _(sp):
            def load_s1(u, slot):
                sp.wait_ge(step_act, at(step_act, QUADS * (u - 1)))
                sp.sem_inc(waited[sp.engine], 1)
                sp.wait_ge(step_dve, at(step_dve, u - 1))
                sp.dma_start(s1_bc[slot][:], s1_rows[bass.ds(u % (NBLK * H), 1), :].rearrange("a n -> (a n)").partition_broadcast(P)
                             ).then_inc(s1_loaded[slot], 16)

            def load_piece(q, slot, row_tile):
                sp.wait_ge(adj_cut, at(adj_cut, q - 1))
                sp.dma_start(adj_in[slot][:], adj_rows[bass.ds(row_tile * P, P), slot * JH * P:(slot + 1) * JH * P]
                             ).then_inc(adj_loaded[slot], 16)

            def load_x(xi, slot, row_tile):
                sp.wait_ge(x_turned, at(x_turned, xi - 1))
                sp.wait_ge(x_maxed, at(x_maxed, xi - 1))
                sp.wait_ge(x_summed, at(x_summed, xi - 1))
                sp.dma_start(x_in[slot][:], x_rows[bass.ds(row_tile * P, P), :]).then_inc(x_loaded[slot], 16)

            def store_block(g):
                sp.wait_ge(y_normed, g + 1)
                sp.dma_start(out_rows[bass.ds((g + NBLK) % NBLK * BLK, BLK), :].rearrange("(t p) f -> p t f", p=P), y[:]
                             ).then_inc(out_stored, 16)

            sp.sem_inc(out_stored, start[out_stored])
            for i in range(JC):
                if i == 2:
                    for fc in range(FC):
                        sp.dma_start(W_sb[:, fc, :].rearrange("p (h o) -> p h o", h=H),
                                     W[:, fc * P:(fc + 1) * P, :].rearrange("h p o -> p h o")).then_inc(w_loaded, 16)
                    for n, a in enumerate((a1, a2)):
                        sp.dma_start(att[:, n, :], a.rearrange("h o -> (h o)").partition_broadcast(P)
                                     ).then_inc(a_loaded, 16)
                if i < PIECES:
                    load_piece(i, i % 2, i // 2)
                load_x(i, i % 2, i)
            for ahead in range(2):
                for later, i in pieces_ahead(0, ahead):
                    load_piece(PIECES + i, i % 2, IT + i // 2)

            with sp.Fori(0, B) as b:
                sp.wait_ge(sT_copied, b + 1)
                for k in range(KB):
                    sp.dma_start(s1_rows[bass.ds((b * KB + k) * H, H), :], sT[32 * k:32 * k + H, :]
                                 ).then_inc(s1_stored, 16)
                sp.wait_ge(s1_stored, 16 * KB * (b + 1))
                load_s1(b * UNITS, 0)
                with sp.Fori(0, KB // 2) as k2:
                    for par in range(2):
                        g = b * KB + k2 * 2 + par
                        for h in range(H):
                            if h == H - 1 and par:
                                with sp.If(k2 < KB // 2 - 1):
                                    load_s1(g * H + h + 1, 0)
                            else:
                                load_s1(g * H + h + 1, (h + 1) % 2)
                            for later, i in pieces_ahead(h, 2):
                                load_piece(PIECES * (g + 1 + later) + i, i % 2,
                                           ((g + 1 + later) * IT + i // 2) % (NBLK * IT))
                            if h % 2 == 0:
                                load_x(JC + IT * g + h // 2, (h // 2) % 2, (JC + IT * g + h // 2) % (NBLK * IT))
                            if h == 5:
                                if par:
                                    store_block(g - 1)
                                else:
                                    with sp.If(g > 0):
                                        store_block(g - 1)
                            if h == 6:
                                sp.wait_ge(w_abs_summed, 1)
                                sp.wait_ge(out_stored, at(out_stored, 16 * g))
                                sp.dma_start(y[:], x_rows[bass.ds(g * BLK, BLK), :].rearrange("(t p) f -> p t f", p=P)
                                             ).then_inc(y_loaded, 16)
            store_block(NBLK - 1)
            sp.wait_ge(out_stored, at(out_stored, 16 * NBLK))
            for slot in range(2):
                sp.wait_ge(adj_loaded[slot], 16 * ((NBLK + 1) * IT + (2 - slot)))
                sp.wait_ge(x_loaded[slot], 16 * (NBLK * IT + JC) // 2)

        @block.tensor
        def _(pe):
            def turn_piece(q, slot):
                pe.wait_ge(piece_copied, at(piece_copied, q - 1))
                pe.wait_ge(adj_cut, at(adj_cut, q + 1))
                bank = ps[:, BANK_T + slot, :].bitcast(BF16)
                for j in range(JH):
                    mm = pe.transpose(bank[:, j * P:(j + 1) * P], adj_bf[slot][:, j * P:(j + 1) * P], ident_bf[:])
                mm.then_inc(piece_turned, 1)

            def turn_x(xi, slot, nth):
                pe.wait_ge(xT_copied, at(xT_copied, xi - 1))
                pe.wait_ge(x_loaded[slot], 16 * (nth + 1))
                for fc in range(FC):
                    mm = pe.transpose(ps[:, BANK_X + slot, fc * P:(fc + 1) * P],
                                      x_in[slot][:, fc * P:(fc + 1) * P], ident[:])
                mm.then_inc(x_turned, 1)

            pe.nop().then_inc(piece_turned, start[piece_turned])
            pe.nop().then_inc(x_turned, start[x_turned])
            pe.nop().then_inc(unit_done, start[unit_done])
            pe.nop().then_inc(pos_summed, start[pos_summed])
            pe.wait_ge(consts_made, 2)
            for i in range(JC):
                if i < PIECES:
                    turn_piece(i, i % 2)
                turn_x(i, i % 2, i // 2)
            pe.wait_ge(w_abs_made, 1)
            for fc in range(FC):
                mm = pe.matmul(ps[:, 0, :], ones[:], y[:, fc, :], start=(fc == 0), stop=(fc == FC - 1))
            mm.then_inc(w_abs_summed, 1)
            pe.wait_ge(wa_made, 1)

            with pe.Fori(0, B) as b:
                pe.wait_ge(xT_copied, at(xT_copied, JC * (b + 1)))
                for fc in range(FC):
                    for k in range(KB):
                        mm = pe.matmul(ps[32 * k:32 * (k + 1), BANK_X, :], wa[:, fc, :], xT[:, fc, k * BLK:(k + 1) * BLK],
                                       start=(fc == 0), stop=(fc == FC - 1))
                mm.then_inc(sT_summed, 1)
                pe.wait_ge(sT_copied, b + 1)
                for t in range(IT):
                    mm = pe.transpose(ps[:, BANK_X + 1, t * P:(t + 1) * P], sT[:, t * P:(t + 1) * P], ident[:])
                mm.then_inc(s_turned, 1)
                for jc in range(JC):
                    if jc == 1:
                        pe.wait_ge(s_col_copied, b + 1)
                    if jc >= 2:
                        pe.wait_ge(hi_d_made, b * JC + jc - 1)
                    for fc in range(FC):
                        mm = pe.matmul(ps[:, BANK_X + jc % 2, :], xT[:, fc, jc * P:(jc + 1) * P], W_sb[:, fc, :],
                                       start=(fc == 0), stop=(fc == FC - 1))
                    mm.then_inc(h_summed, 1)
                    if jc == 2:
                        pe.wait_ge(x_summed, at(x_summed, JC * (b + 1)))
                        pe.wait_ge(unit_read, at(unit_read, UNITS * b - 1))
                        for fc in range(FC):
                            mm = pe.matmul(ps[:, 0, fc:fc + 1], x_sum[:, fc * P:(fc + 1) * P], ones[:, 0:1],
                                           start=True, stop=True)
                        mm.then_inc(x_sum_turned, 1)
                    if jc == 5:
                        pe.wait_ge(x_sum_spread, b + 1)
                        pe.wait_ge(piece_copied, at(piece_copied, PIECES * (b * KB + 1)))
                        for fc in range(FC):
                            mm = pe.matmul(ps[:, BANK_T, :], x_sum_bc[:, fc * P:(fc + 1) * P], W_sb[:, fc, :],
                                           start=(fc == 0), stop=(fc == FC - 1))
                        mm.then_inc(h_mean_summed, 1)
                with pe.Fori(0, KB // 2) as k2:
                    for par in range(2):
                        g = b * KB + k2 * 2 + par
                        for h in range(H):
                            u = g * H + h
                            for i in PIECES_OF[h]:
                                turn_piece(PIECES * (g + 1) + i, i % 2)
                            hp = h % 2
                            if h == 0 and par == 0:
                                pe.wait_ge(tiny_made, b + 1)
                                pe.wait_ge(lo_made, at(lo_made, 2 * JC * (b + 1) - 1))
                            pe.wait_ge(pos_made, at(pos_made, QUADS * (u + 1)))
                            pe.wait_ge(unit_read, at(unit_read, u - 1))
                            for it in range(IT):
                                acc = ps[:, 2 * hp, it * O1:(it + 1) * O1]
                                pe.matmul(acc, ones_bf[:], tiny[:, h, :], start=True, stop=False)
                                for j in range(JC):
                                    mask = m_pos[hp][:, j, it * P:(it + 1) * P]
                                    pe.matmul(acc, mask, b_hi[:, j, h, :], start=False, stop=False)
                                    mm = pe.matmul(acc, mask, b_lo[:, j, h, :], start=False, stop=(j == JC - 1))
                            mm.then_inc(pos_summed, 1)
                            if h == 0 and par == 0:
                                pe.wait_ge(lo_made, at(lo_made, 2 * JC * (b + 1)))
                            if h % 2 == 0:
                                turn_x(JC + IT * g + h // 2, (h // 2) % 2, JC // 2 + g * (IT // 2) + h // 4)
                            pe.wait_ge(neg_made, at(neg_made, QUADS * (u + 1)))
                            pe.sem_inc(waited[pe.engine], 1)
                            for it in range(IT):
                                acc = ps[:, 2 * hp + 1, it * O1:(it + 1) * O1]
                                for j in range(JC):
                                    mask = m_neg[hp][:, j, it * P:(it + 1) * P]
                                    pe.matmul(acc, mask, d_hi[:, j, h, :], start=(j == 0), stop=False)
                                    mm = pe.matmul(acc, mask, d_lo[:, j, h, :], start=False, stop=(j == JC - 1))
                            mm.then_inc(unit_done, 1)

        @block.scalar
        def _(act):
            def copy_piece(q, slot, buf, it):
                act.wait_ge(piece_turned, at(piece_turned, q + 1))
                act.sem_inc(waited[act.engine], 1)
                bank = ps[:, BANK_T + slot, :].bitcast(BF16).rearrange("p (j i) -> p j i", j=JH)
                nc.scalar.activation(maskT[buf][:, slot * JH:(slot + 1) * JH, it * P:(it + 1) * P], bank, ACT.Copy,
                                     saturate=False).then_inc(piece_copied, 1)

            def copy_xT(xi, slot, col):
                act.wait_ge(x_turned, at(x_turned, xi + 1))
                bank = ps[:, BANK_X + slot, :].rearrange("p (c n) -> p c n", c=FC)
                nc.scalar.activation(xT[:, :, bass.ds(col, P)], bank, ACT.Copy).then_inc(xT_copied, 1)

            def compare(u, h, nth):
                act.wait_ge(s1_loaded[h % 2], 16 * (nth + 1))
                for qd in range(QUADS):
                    act.wait_ge(pos_made, at(pos_made, QUADS * (u - 1) + qd + 1))
                    act.sem_inc(waited[act.engine], 1)
                    for c in range(JQ):
                        if c not in DVE_SLOTS.get(qd, ()):
                            j = qd * JQ + c
                            ins = nc.scalar.activation(step[qd][:, c, :], s1_bc[h % 2][:], ACT.Relu,
                                                       bias=s2_steep[:, j, h:h + 1], scale=STEEP, saturate=False)
                    ins.then_inc(step_act, 1)

            act.nop().then_inc(piece_copied, start[piece_copied])
            act.nop().then_inc(xT_copied, start[xT_copied])
            act.nop().then_inc(step_act, start[step_act])
            for i in range(JC):
                if i < PIECES:
                    copy_piece(i, i % 2, 0, i // 2)
                copy_xT(i, i % 2, i * P)

            with act.Fori(0, B) as b:
                act.wait_ge(sT_summed, b + 1)
                nc.scalar.activation(sT[:], ps[:, BANK_X, :], ACT.Copy).then_inc(sT_copied, 1)
                act.wait_ge(s_rel_made, b + 1)
                nc.scalar.activation(e_b[:], s2_rel[:], ACT.Exp)
                nc.scalar.activation(e_d[:], s2_rel[:], ACT.Exp, scale=SLOPE)
                nc.scalar.activation(r_row[:], r_in[:], ACT.Exp, scale=SLOPE - 1.0).then_inc(exp_made, 1)
                compare(b * UNITS, 0, b * (UNITS // 2))
                with act.Fori(0, KB // 2) as k2:
                    for par in range(2):
                        g = b * KB + k2 * 2 + par
                        for h in range(H):
                            u = g * H + h
                            for i in PIECES_OF[h - 1] if h else ():
                                act.wait_ge(neg_made, at(neg_made, QUADS * H * g))
                                copy_piece(PIECES * (g + 1) + i, i % 2, 1 - par, i // 2)
                            if h % 2 == 1:
                                t = h // 2
                                act.wait_ge(h_summed, JC * (b + 1))
                                copy_xT(JC + IT * g + t, t % 2, k2 * (2 * BLK) + par * BLK + t * P)
                            if h == H - 1 and par:
                                with act.If(k2 < KB // 2 - 1):
                                    compare(u + 1, 0, (g + 1) * (H // 2))
                            else:
                                compare(u + 1, (h + 1) % H, g * (H // 2) + (h + 1) // 2)

        @block.vector
        def _(dve):
            V = nc.vector

            def max_x(xi, slot, nth, col):
                dve.wait_ge(x_loaded[slot], 16 * (nth + 1))
                V.tensor_reduce(xmax[:, bass.ds(col, 1)], x_in[slot][:], AX.X, ALU.max,
                                apply_absolute_value=True).then_inc(x_maxed, 1)

            def take_unit(u, h, it0):
                hp = h % 2
                pos = ps[:, 2 * hp, 0:IT * O1].rearrange("p (t c) -> p t c", t=IT)
                neg = ps[:, 2 * hp + 1, 0:IT * O1].rearrange("p (t c) -> p t c", t=IT)
                r = r_row[:, bass.ds(it0, IT), h:h + 1].to_broadcast([P, IT, O1])
                dve.wait_ge(unit_done, at(unit_done, u + 1))
                V.tensor_tensor(neg_part[:], neg, r, ALU.mult).then_inc(neg_scaled, 1)
                dve.wait_ge(neg_scaled, u + 1)
                dve.wait_ge(att_made, at(att_made, u - 1))
                V.tensor_tensor(total[hp][:], pos, neg_part[:], ALU.add).then_inc(unit_read, 1)
                dve.wait_ge(unit_read, at(unit_read, u + 1))
                V.reciprocal(den_inv[hp][:], total[hp][:, :, O]).then_inc(den_inverted, 1)

            def ln_first_half(g):
                dve.wait_ge(y_made, at(y_made, 2 * g + 1))
                for t in range(IT // 2):
                    V.bn_stats(ln_stats[:, t, :], y[:, t, :])

            def ln_statistics(g):
                dve.wait_ge(y_made, at(y_made, 2 * (g + 1)))
                for t in range(IT // 2, IT):
                    ins = V.bn_stats(ln_stats[:, t, :], y[:, t, :])
                ins.then_inc(ln_stats_made, 1)
                dve.wait_ge(ln_stats_made, g + 1)
                dve.sem_inc(waited[dve.engine], 1)
                for t in range(IT):
                    ins = V.bn_aggr(ln_mv[:, t, :], ln_stats[:, t, :])
                ins.then_inc(ln_mv_made, 1)
                dve.wait_ge(ln_mv_made, g + 1)
                V.tensor_scalar(ln_var[:], ln_mv[:, :, 1], EPS_LN, None, ALU.add).then_inc(ln_var_made, 1)

            def ln_apply(g):
                dve.wait_ge(ln_rstd_made, g + 1)
                for t in range(IT):
                    ins = V.tensor_scalar(y[:, t, :], y[:, t, :], ln_mv[:, t, 0:1], ln_rstd[:, t:t + 1],
                                          ALU.subtract, ALU.mult)
                ins.then_inc(y_normed, 1)

            V.nop().then_inc(x_maxed, start[x_maxed])
            V.nop().then_inc(step_dve, start[step_dve])
            V.nop().then_inc(pos_made, start[pos_made])
            V.nop().then_inc(neg_made, start[neg_made])
            V.nop().then_inc(unit_read, start[unit_read])
            V.nop().then_inc(adj_cut, start[adj_cut])
            V.memset(ones_bf[:], 1.0)
            V.memset(wa[:], 0.0)
            V.memset(tiny_f[:], TINY * SPLIT_TOP).then_inc(setup_step, 1)
            dve.wait_ge(ident_made, 1)
            V.tensor_copy(ident_bf[:], ident[:]).then_inc(consts_made, 1)
            for i in range(JC):
                if i < PIECES:
                    dve.wait_ge(adj_loaded[i % 2], 16 * (i // 2 + 1))
                    if i >= 2:
                        dve.wait_ge(piece_turned, at(piece_turned, i - 1))
                    V.tensor_scalar(adj_bf[i % 2][:], adj_in[i % 2][:], 0.0, None, ALU.is_gt).then_inc(adj_cut, 1)
                max_x(i, i % 2, i // 2, i)
                if i == 4:
                    dve.wait_ge(w_loaded, 16 * FC)
                    dve.wait_ge(a_loaded, 32)
                if 4 <= i < 8:
                    fc = i - 4
                    ins = V.scalar_tensor_tensor(out=y[:, fc, :], in0=W_sb[:, fc, :], scalar=-1.0, in1=W_sb[:, fc, :],
                                                 op0=ALU.mult, op1=ALU.max)
                    if fc == FC - 1:
                        ins.then_inc(w_abs_made, 1)
                if i >= 8:
                    n, fc = divmod(i - 8, FC)
                    done = 1 + 2 * (i - 8)
                    dve.wait_ge(setup_step, done)
                    V.tensor_tensor(prod[:], W_sb[:, fc, :], att[:, n, :], ALU.mult).then_inc(setup_step, 1)
                    dve.wait_ge(setup_step, done + 1)
                    V.tensor_reduce(wa[:, fc, n * H:(n + 1) * H], prod[:].rearrange("p (h o) -> p h o", h=H),
                                    AX.X, ALU.add).then_inc(setup_step, 1)
            dve.wait_ge(setup_step, 1 + 2 * 2 * FC)
            V.nop().then_inc(wa_made, 1)
            dve.wait_ge(w_abs_summed, 1)
            V.tensor_reduce(w_norm[:], ps[:, 0, :], AX.X, ALU.max)

            def batch_start(b):
                dve.wait_ge(s_turned, b + 1)
                V.tensor_copy(s_col[:].rearrange("p (k t) s -> p t k s", t=IT),
                              ps[:, BANK_X + 1, :].rearrange("p (t k s) -> p t k s", t=IT, k=KB)[:, :, :, 0:2 * H]
                              ).then_inc(s_col_copied, 1)
                dve.wait_ge(s_col_copied, b + 1)
                dve.wait_ge(x_maxed, at(x_maxed, JC * (b + 1)))
                s1 = s_col[:, :, 0:H]
                s2 = s_col[:, :, H:2 * H]
                V.tensor_reduce(stat[:, 0:H], s2.rearrange("p j k -> p k j"), AX.X, ALU.max)
                V.tensor_reduce(stat[:, H:H + 1], xmax[:], AX.X, ALU.max).then_inc(stat_made, 1)
                V.tensor_scalar(s2_steep[:], s2, STEEP, None, ALU.mult)
                dve.wait_ge(stat_spread, b + 1)
                top = stat_all[:, 0:H].unsqueeze(1).to_broadcast([P, JC, H])
                V.tensor_tensor(s2_rel[:], s2, top, ALU.subtract)
                V.tensor_tensor(r_in[:], s1, top, ALU.add).then_inc(r_sum_made, 1)
                V.tensor_scalar(bound[:], stat_all[:, H:H + 1], w_norm[:, 0:1], 1e-20, ALU.mult, ALU.max
                                ).then_inc(bound_step, 1)
                dve.wait_ge(r_sum_made, b + 1)
                V.tensor_scalar(r_in[:], r_in[:], 0.0, None, ALU.max).then_inc(s_rel_made, 1)
                dve.wait_ge(bound_step, 3 * b + 1)
                V.reciprocal(bound_inv[:], bound[:]).then_inc(bound_step, 1)
                dve.wait_ge(bound_step, 3 * b + 2)
                V.tensor_scalar(kappa[:], bound_inv[:], SPLIT_TOP, None, ALU.mult)
                V.tensor_scalar(kappa_tiny[:], bound_inv[:], SPLIT_TOP * TINY / N, None, ALU.mult
                                ).then_inc(bound_step, 1)
                dve.wait_ge(bound_step, 3 * b + 3)
                dve.wait_ge(exp_made, b + 1)
                V.tensor_scalar(b_hi[:, :, :, O], e_b[:], SPLIT_TOP, None, ALU.mult)
                V.tensor_scalar(d_hi[:, :, :, O], e_d[:], SPLIT_TOP, None, ALU.mult).then_inc(den_hi_made, 1)
                V.tensor_scalar(k_b[:], e_b[:], kappa[:, 0:1], None, ALU.mult)
                V.tensor_scalar(k_d[:], e_d[:], kappa[:, 0:1], None, ALU.mult).then_inc(k_made, 1)
                dve.wait_ge(den_hi_made, b + 1)
                V.scalar_tensor_tensor(out=b_lo[:, :, :, O], in0=e_b[:], scalar=SPLIT_TOP, in1=b_hi[:, :, :, O],
                                       op0=ALU.mult, op1=ALU.subtract)
                V.scalar_tensor_tensor(out=d_lo[:, :, :, O], in0=e_d[:], scalar=SPLIT_TOP, in1=d_hi[:, :, :, O],
                                       op0=ALU.mult, op1=ALU.subtract)
                dve.wait_ge(k_made, b + 1)

            def split_chunk(b, jc):
                bank = ps[:, BANK_X + jc % 2, :].rearrange("p (h o) -> p h o", h=H)
                full_b = prod[:].rearrange("p (h o) -> p h o", h=H)
                full_d = prod_d[:].rearrange("p (h o) -> p h o", h=H)
                kb = k_b[:, jc, :].unsqueeze(2).to_broadcast([P, H, O])
                kd = k_d[:, jc, :].unsqueeze(2).to_broadcast([P, H, O])
                dve.wait_ge(h_summed, b * JC + jc + 1)
                V.tensor_tensor(b_hi[:, jc, :, 0:O], bank, kb, ALU.mult)
                dve.wait_ge(lo_made, at(lo_made, 2 * JC * b + 2 * jc - 1))
                V.tensor_tensor(full_b, bank, kb, ALU.mult).then_inc(hi_b_made, 1)
                V.tensor_tensor(d_hi[:, jc, :, 0:O], bank, kd, ALU.mult)
                dve.wait_ge(lo_made, at(lo_made, 2 * JC * b + 2 * jc))
                V.tensor_tensor(full_d, bank, kd, ALU.mult).then_inc(hi_d_made, 1)

            def no_edge_start(b):
                dve.wait_ge(h_mean_summed, b + 1)
                V.tensor_scalar(tiny_f[:, :, 0:O], ps[:, BANK_T, :].rearrange("p (h o) -> p h o", h=H),
                                kappa_tiny[:, 0:1], None, ALU.mult)
                V.memset(tiny_f[:, :, O:O1], TINY * SPLIT_TOP).then_inc(tiny_step, 1)
                dve.wait_ge(tiny_step, 6 * b + 1)

            def no_edge_part(b, part):
                V.tensor_copy(tiny_part[:], tiny_f[:]).then_inc(tiny_step, 1)
                dve.wait_ge(tiny_step, 6 * b + 2 + 2 * part)
                if part == 0:
                    V.tensor_scalar(tiny[:], tiny_part[:], ident[:, 0:1], None, ALU.mult)
                else:
                    ins = V.scalar_tensor_tensor(out=tiny[:], in0=tiny_part[:], scalar=ident[:, part:part + 1],
                                                 in1=tiny[:], op0=ALU.mult, op1=ALU.add)
                if part < 2:
                    V.tensor_tensor(tiny_f[:], tiny_f[:], tiny_part[:], ALU.subtract).then_inc(tiny_step, 1)
                    dve.wait_ge(tiny_step, 6 * b + 3 + 2 * part)
                else:
                    ins.then_inc(tiny_made, 1)

            def compare(h, nth):
                hp = h % 2
                dve.wait_ge(s1_loaded[hp], 16 * (nth + 1))
                dve.sem_inc(waited[dve.engine], 1)
                for qd, chunks in DVE_SLOTS.items():
                    for c in chunks:
                        j = qd * JQ + c
                        ins = V.tensor_scalar(step[qd][:, c, :], s1_bc[hp][:], s_col[:, j, H + h:H + h + 1],
                                              0.0, ALU.add, ALU.is_gt, saturate=False)
                ins.then_inc(step_dve, 1)

            def make_pos(u, h, mask, qd, first_of_block=None):
                hp = h % 2
                if qd == 0:
                    if first_of_block is not None:
                        dve.wait_ge(piece_copied, at(piece_copied, PIECES * (first_of_block + 1)))
                    dve.wait_ge(pos_summed, at(pos_summed, u - 1))
                    dve.wait_ge(step_dve, at(step_dve, u + 1))
                dve.wait_ge(step_act, at(step_act, QUADS * u + qd + 1))
                js = slice(qd * JQ, (qd + 1) * JQ)
                V.tensor_tensor(words(m_pos[hp][:, js, :]), words(step[qd][:]),
                                words(mask[:, js, :]), ALU.bitwise_and).then_inc(pos_made, 1)

            def make_neg(u, h, mask, qd):
                hp = h % 2
                if qd == 0:
                    dve.wait_ge(unit_done, at(unit_done, u - 1))
                js = slice(qd * JQ, (qd + 1) * JQ)
                dve.wait_ge(pos_made, at(pos_made, QUADS * u + qd + 1))
                V.tensor_tensor(words(m_neg[hp][:, js, :]), words(m_pos[hp][:, js, :]),
                                words(mask[:, js, :]), ALU.bitwise_xor).then_inc(neg_made, 1)

            def make_masks(u, h, mask, nth, first_of_block=None):
                compare(h, nth)
                for qd in range(QUADS):
                    make_pos(u, h, mask, qd, first_of_block)
                for qd in range(QUADS):
                    make_neg(u, h, mask, qd)

            with dve.Fori(0, B) as b:
                batch_start(b)
                for jc in range(JC):
                    split_chunk(b, jc)
                    if jc == 3:
                        dve.wait_ge(x_sum_turned, b + 1)
                        for fc in range(FC):
                            ins = V.tensor_scalar(x_sum_bc[:, fc * P:(fc + 1) * P], ones[:], ps[:, 0, fc:fc + 1], None,
                                                  ALU.mult)
                        ins.then_inc(x_sum_spread, 1)
                    if jc == 1:
                        compare(0, b * (UNITS // 2))
                    if 4 <= jc < 4 + QUADS:
                        make_pos(b * UNITS, 0, maskT[0], jc - 4, b * KB)
                    if 8 <= jc < 8 + QUADS:
                        make_neg(b * UNITS, 0, maskT[0], jc - 8)
                    if jc == 11:
                        no_edge_start(b)
                    if 12 <= jc < 15:
                        no_edge_part(b, jc - 12)
                with dve.Fori(0, KB // 2) as k2:
                    for par in range(2):
                        g = b * KB + k2 * 2 + par
                        for h in range(H):
                            u = g * H + h
                            if h % 2 == 0:
                                t = h // 2
                                max_x(JC + IT * g + t, t % 2, JC // 2 + g * (IT // 2) + h // 4,
                                      k2 * (2 * IT) + par * IT + t)
                            if h < H - 1:
                                make_masks(u + 1, h + 1, maskT[par], g * (H // 2) + (h + 1) // 2)
                            elif par == 0:
                                make_masks(u + 1, 0, maskT[1], (g + 1) * (H // 2), g + 1)
                            else:
                                with dve.If(k2 < KB // 2 - 1):
                                    make_masks(u + 1, 0, maskT[0], (g + 1) * (H // 2), g + 1)
                            take_unit(u, h, k2 * (2 * IT) + par * IT)
                            for when, work in ((1, ln_first_half), (2, ln_statistics), (3, ln_apply)):
                                if h == when:
                                    if par:
                                        work(g - 1)
                                    else:
                                        with dve.If(g > 0):
                                            work(g - 1)
            ln_first_half(NBLK - 1)
            ln_statistics(NBLK - 1)
            ln_apply(NBLK - 1)

        @block.gpsimd
        def _(pool):
            G = nc.gpsimd

            def add_x(xi, slot, nth):
                pool.wait_ge(x_summed, at(x_summed, xi))
                pool.wait_ge(x_loaded[slot], 16 * (nth + 1))
                G.tensor_tensor(x_sum[:], x_sum[:], x_in[slot][:], ALU.add).then_inc(x_summed, 1)

            def cut_piece(q, slot, nth):
                pool.wait_ge(adj_loaded[slot], 16 * (nth + 1))
                pool.sem_inc(waited[pool.engine], 1)
                pool.wait_ge(piece_turned, at(piece_turned, q - 1))
                pool.sem_inc(waited[pool.engine], 1)
                G.tensor_scalar(adj_bf[slot][:], adj_in[slot][:], 0.0, None, ALU.is_gt).then_inc(adj_cut, 1)

            def deviation(g):
                pool.wait_ge(ln_var_made, g + 1)
                G.tensor_tensor(ln_rstd[:], ln_var[:], minus_half[:], ALU.pow).then_inc(ln_rstd_made, 1)

            def divide_unit(u, h, nth_y):
                hp = h % 2
                pool.wait_ge(den_inverted, u + 1)
                G.tensor_tensor(den_scaled[hp][:], den_inv[hp][:], bound[:].to_broadcast([P, IT]), ALU.mult
                                ).then_inc(den_made, 1)
                if h == 0:
                    pool.wait_ge(y_made, at(y_made, 2 * nth_y))
                pool.wait_ge(den_made, u + 1)
                G.tensor_tensor(att[:, :, h * O:(h + 1) * O], total[hp][:, :, 0:O],
                                den_scaled[hp][:].unsqueeze(2).to_broadcast([P, IT, O]), ALU.mult).then_inc(att_made, 1)

            def residual(g):
                pool.wait_ge(y_loaded, 16 * (g + 1))
                pool.wait_ge(att_made, at(att_made, UNITS // KB * (g + 1)))
                for half in range(2):
                    t = slice(half * IT // 2, (half + 1) * IT // 2)
                    G.tensor_tensor(y[:, t, :], y[:, t, :], att[:, t, :], ALU.add).then_inc(y_made, 1)

            G.memset(ones[:], 1.0)
            G.memset(minus_half[:], -0.5)
            G.memset(x_sum[:], 0.0)
            G.memset(ident[:], 0.0).then_inc(ident_step, 1)
            pool.wait_ge(ident_step, 1)
            G.affine_select(out=ident[:], in_=ident[:], compare_op=ALU.not_equal, fill=1.0, base=0,
                            pattern=[[-1, P]], channel_multiplier=1).then_inc(ident_made, 1)
            pool.wait_ge(ident_made, 1)
            G.nop().then_inc(consts_made, 1)
            G.nop().then_inc(x_summed, start[x_summed])
            G.nop().then_inc(att_made, start[att_made])
            G.nop().then_inc(lo_made, start[lo_made])
            G.nop().then_inc(y_made, start[y_made])
            for i in range(JC):
                add_x(i, i % 2, i // 2)
            for later, i in pieces_ahead(0, 0):
                cut_piece(PIECES + i, i % 2, IT + i // 2)

            with pool.Fori(0, B) as b:
                pool.wait_ge(stat_made, b + 1)
                pool.sem_inc(waited[pool.engine], 1)
                G.partition_all_reduce(stat_all[:], stat[:], P, RMAX).then_inc(stat_spread, 1)
                for jc in range(JC):
                    full_b = prod[:].rearrange("p (h o) -> p h o", h=H)
                    full_d = prod_d[:].rearrange("p (h o) -> p h o", h=H)
                    pool.wait_ge(hi_b_made, b * JC + jc + 1)
                    G.tensor_tensor(b_lo[:, jc, :, 0:O], full_b, b_hi[:, jc, :, 0:O], ALU.subtract).then_inc(lo_made, 1)
                    pool.wait_ge(hi_d_made, b * JC + jc + 1)
                    G.tensor_tensor(d_lo[:, jc, :, 0:O], full_d, d_hi[:, jc, :, 0:O], ALU.subtract).then_inc(lo_made, 1)
                    if jc == 4:
                        pool.wait_ge(x_sum_turned, b + 1)
                        pool.sem_inc(waited[pool.engine], 1)
                        G.memset(x_sum[:], 0.0).then_inc(x_sum_cleared, 1)
                pool.wait_ge(x_sum_cleared, b + 1)
                pool.sem_inc(waited[pool.engine], 1)
                with pool.Fori(0, KB // 2) as k2:
                    for par in range(2):
                        g = b * KB + k2 * 2 + par
                        for h in range(H):
                            for later, i in pieces_ahead(h, 1):
                                cut_piece(PIECES * (g + 1 + later) + i, i % 2, (g + 1 + later) * IT + i // 2)
                            if h % 2 == 0:
                                t = h // 2
                                add_x(JC + IT * g + t, t % 2, JC // 2 + g * (IT // 2) + t // 2)
                            if h == 3:
                                if par:
                                    deviation(g - 1)
                                else:
                                    with pool.If(g > 0):
                                        deviation(g - 1)
                            if h == 0:
                                if par:
                                    residual(g - 1)
                                else:
                                    with pool.If(g > 0):
                                        residual(g - 1)
                            else:
                                divide_unit(g * H + h - 1, h - 1, g)
                            if h == H - 1:
                                divide_unit(g * H + h, h, g)
            residual(NBLK - 1)
            deviation(NBLK - 1)


_INS = ["x", "adj", "L0_gnn_W", "L0_gnn_a1", "L0_gnn_a2"]


def kernel(**inputs):
    import numpy as _np
    import concourse.bacc as _bacc
    from concourse import mybir as _mybir
    from concourse.bass_utils import run_bass_kernel_spmd as _run

    nc = _bacc.Bacc("TRN2", target_bir_lowering=False, num_devices=1, dynamic_dma_scratch_size=1024)
    arrays, args = {}, []
    for name in _INS:
        a = _np.ascontiguousarray(inputs[name])
        arrays[f"in_{name}"] = a
        args.append(nc.dram_tensor(f"in_{name}", a.shape, _mybir.dt.from_np(a.dtype), kind="ExternalInput").ap())
    shape = arrays["in_x"].shape
    args.append(nc.dram_tensor("out_0", shape, _mybir.dt.float32, kind="ExternalOutput").ap())
    gat_kernel(nc, *args)
    r = _run(nc, [arrays], core_ids=[0])
    return r.results[0]["out_0"]
```
